# Optimizing a Trainium2 kernel written in Bass

```python
import numpy as np
import jax
import jax.numpy as jnp

def _softmax(x, axis=-1):
    return jax.nn.softmax(x, axis=axis)

def _gelu(x):
    return jax.nn.gelu(x, approximate=True)

def _silu(x):
    return jax.nn.silu(x)

def _sigmoid(x):
    return jax.nn.sigmoid(x)

def _layernorm(x, axis=-1, eps=1e-05):
    m = jnp.mean(x, axis=axis, keepdims=True)
    v = jnp.var(x, axis=axis, keepdims=True)
    return (x - m) / jnp.sqrt(v + eps)

def _scatter_add(tgt, idx, src, axis=0):
    return tgt.at[idx].add(src)

def _segment_sum(src, seg, n):
    return jax.ops.segment_sum(src, seg, n)
kernel_name = 'mk_gnn_resnorm_d1_gnn_r8_b42399'

def setup_inputs(seed: int=0):
    np.random.seed(seed)
    _w = jnp.asarray

    def _rec_inputs():
        import jax
        import jax.numpy as jnp
        _gk = jax.random.key(seed)
        x = -0.000202 + 1 * jax.random.normal(jax.random.fold_in(_gk, 1), (12500, 128), jnp.float32)
        _s = jax.random.randint(jax.random.fold_in(_gk, 2), (200000,), 0, 12500, jnp.int32)
        _d = jax.random.randint(jax.random.fold_in(_gk, 3), (200000,), 0, 12500, jnp.int32)
        _loop = jnp.arange(12500, dtype=jnp.int32)
        src = jnp.concatenate([_s, _d, _loop])
        dst = jnp.concatenate([_d, _s, _loop])
        _o = jnp.argsort(dst, stable=True)
        src = src[_o]
        dst = dst[_o]
        return (x, src, dst)
    x, src, dst = _rec_inputs()

    def _L0_gnn_setup():
        import jax, jax.numpy as jnp
        import numpy as np
        N_NODES = 6250
        N_EDGES = 100000
        IN_FEAT = 128
        OUT_FEAT = 128
        key = jax.random.key(seed)
        ks = jax.random.split(key, 9)
        s = 1.0 / np.sqrt(IN_FEAT)
        return {'x': jax.random.normal(ks[0], (N_NODES, IN_FEAT), dtype=jnp.float32), 'src': jax.random.randint(ks[1], (N_EDGES,), 0, N_NODES), 'dst': jax.random.randint(ks[2], (N_EDGES,), 0, N_NODES), 'W1': jax.random.uniform(ks[3], (IN_FEAT, OUT_FEAT), jnp.float32, -s, s), 'b1': jax.random.uniform(ks[4], (OUT_FEAT,), jnp.float32, -s, s), 'W2': jax.random.uniform(ks[5], (OUT_FEAT, 1), jnp.float32, -s, s), 'b2': jax.random.uniform(ks[6], (1,), jnp.float32, -s, s), 'W4': jax.random.uniform(ks[7], (IN_FEAT, OUT_FEAT), jnp.float32, -s, s), 'b4': jax.random.uniform(ks[8], (OUT_FEAT,), jnp.float32, -s, s)}
    _L0_gnn_all = _L0_gnn_setup()
    _L0_gnn_in = {k: v for k, v in _L0_gnn_all.items() if k in ('W1', 'b1', 'W2', 'b2', 'W4', 'b4')}
    del _L0_gnn_all
    return {'x': x, 'src': src, 'dst': dst, 'L0_gnn_W1': _L0_gnn_in['W1'], 'L0_gnn_b1': _L0_gnn_in['b1'], 'L0_gnn_W2': _L0_gnn_in['W2'], 'L0_gnn_b2': _L0_gnn_in['b2'], 'L0_gnn_W4': _L0_gnn_in['W4'], 'L0_gnn_b4': _L0_gnn_in['b4']}

def reference(x, src, dst, L0_gnn_W1, L0_gnn_b1, L0_gnn_W2, L0_gnn_b2, L0_gnn_W4, L0_gnn_b4):
    import jax
    import jax.numpy as jnp

    def _L0_gnn_ref(x, src, dst, W1, b1, W2, b2, W4, b4):
        import jax, jax.numpy as jnp
        import numpy as np
        N_NODES = 6250
        N_EDGES = 100000
        IN_FEAT = 128
        OUT_FEAT = 128
        n_nodes = x.shape[0]
        theta = x[dst] - x[src]
        w = jax.nn.sigmoid(jax.nn.relu(theta @ W1 + b1) @ W2 + b2)
        w_theta = w * theta
        agg = jax.ops.segment_sum(w_theta, dst, num_segments=n_nodes)
        indeg = jax.ops.segment_sum(jnp.ones((dst.shape[0], 1), x.dtype), dst, num_segments=n_nodes)
        return agg + indeg * (x @ W4 + b4)
    x = _layernorm(x + _L0_gnn_ref(x, src, dst, L0_gnn_W1, L0_gnn_b1, L0_gnn_W2, L0_gnn_b2, L0_gnn_W4, L0_gnn_b4), axis=-1)
    return x

_drawn_inputs = setup_inputs


def setup_inputs(seed=0):
    import zlib

    import numpy as np

    out = dict(_drawn_inputs(seed))
    spreads = {}
    factors = {'L0_gnn_b1': 26.638}
    for name, (base, spread) in spreads.items():
        noise = np.random.default_rng([zlib.crc32(name.encode()), seed]).standard_normal(out[name].shape)
        drawn = base * np.exp(spread * noise) if base else spread * noise
        out[name] = jnp.asarray(drawn.astype(out[name].dtype))
    for name, factor in factors.items():
        out[name] = (out[name] * factor).astype(out[name].dtype)
    return out
```

```python
import concourse.bass as bass
from concourse import mybir
from contextlib import ExitStack

FP32 = mybir.dt.float32
BF16 = mybir.dt.bfloat16
I32 = mybir.dt.int32
ALU = mybir.AluOpType
ACT = mybir.ActivationFunctionType
AX = mybir.AxisListType

P = 128
F = 128
EPS = 1e-5


class Sizes:

    def __init__(self, nodes, edges):
        self.nodes, self.edges = nodes, edges
        self.chunks = edges // CHUNK
        left = edges - self.chunks * CHUNK
        self.tail_parts = left // B
        self.last_base = nodes - P
        assert left == self.tail_parts * B and 0 < self.tail_parts <= P
        assert self.chunks % 2 == 1 and self.chunks >= 5
        self.gp = max(n for n in range(1, P) if edges % (n * GU) == 0 and nodes % (n * GU) == 0)
        self.edge_turns = edges // (self.gp * GU)
        self.node_tiles = nodes // self.gp


B = 4
NB = 7
K = B * NB
CHUNK = K * P
GW = 144
ZR = 10
GU = 4


class Chunk:

    def __init__(self, c, parity, nth):
        self.c, self.parity, self.nth = c, parity, nth


class Chain:

    def __init__(self, eng, sem, before):
        self.eng, self.sem, self.count = eng, sem, before

    def __call__(self, ins):
        ins.then_inc(self.sem, 1)
        self.count = self.count + 1
        self.eng.wait_ge(self.sem, self.count)


def wait(eng, sem, value):
    if not (isinstance(value, int) and value <= 0):
        eng.wait_ge(sem, value)


def build(nc, x, src, dst, W1, b1, W2, b2, W4, b4, out):
    z = Sizes(x.shape[0], src.shape[0])
    with ExitStack() as ctx:
        def sb(name, shape, dt=FP32):
            return ctx.enter_context(nc.sbuf_tensor(name, shape, dt))

        def ps(name, shape, dt=FP32):
            return ctx.enter_context(nc.psum_tensor(name, shape, dt))

        def sem(name):
            return ctx.enter_context(nc.semaphore(name))

        acc = nc.dram_tensor("acc", (z.nodes + P, F + 1), FP32, kind="Internal").ap()

        w14 = sb("w14", [P, 2 * F])
        neg_w1 = sb("neg_w1", [P, F])
        w2 = sb("w2", [P, 1])
        b1_col = sb("b1_col", [P, 1])
        b2_col = sb("b2_col", [P, 1])
        b4_rows = sb("b4_rows", [P, F])
        ones_col = sb("ones_col", [P, 1])
        ident = sb("ident", [P, P])
        ident_bf = sb("ident_bf", [P, P], BF16)
        col_minus_row = sb("col_minus_row", [P, P])
        col_no = sb("col_no", [P, P])
        row_no = sb("row_no", [P, 1])
        before = sb("before", [P, P])
        src_i = sb("src_i", [P, 2, K], I32)
        dst_i = sb("dst_i", [P, 2, K], I32)
        first_i = sb("first_i", [P, 2, 1], I32)
        base_i = sb("base_i", [P, 2, 1], I32)
        base_f = sb("base_f", [P, 2, 1])
        rel = sb("rel", [P, 2, K])
        rel_bf = sb("rel_bf", [P, 2, K], BF16)
        delta = sb("delta", [P, 1])
        step_back = sb("step_back", [P, 1])
        step_far = sb("step_far", [P, 1])
        bad = sb("bad", [P, 1])
        carry_sel = sb("carry_sel", [P, 2, P])
        window = sb("window", [P, 2, F])
        part = sb("part", [P, 2, 3, F], BF16)
        rest = sb("rest", [P, F])
        gath = sb("gath", [P, K, GW])
        hot_ne = sb("hot_ne", [P, 2, B * P], BF16)
        hot_en = sb("hot_en", [P, 2, B, P])
        srcT = sb("srcT", [P, 2, B * P])
        hidden = sb("hidden", [P, 2, B * P])
        wgt = sb("wgt", [P, 2, B])
        deg = sb("deg", [P, 2, NB])
        sums = sb("sums", [P, F + 2])
        placed = sb("placed", [P, 1])
        deg_own = sb("deg_own", [P, 1])
        winT = sb("winT", [P, P])
        sw1 = sb("sw1", [P, 1])
        lin = sb("lin", [P, 2, F])
        mix = sb("mix", [P, F])
        y = sb("y", [P, F])
        stats = sb("stats", [P, 6])
        mv = sb("mv", [P, 2])
        var = sb("var", [P, 1])
        neg_half = sb("neg_half", [P, 1])
        bits = sb("bits", [P, 1], I32)
        square = sb("square", [P, 1])
        rstd = sb("rstd", [P, 1])
        yout = sb("yout", [P, F])
        out_base = sb("out_base", [P, 2, 1], I32)
        g_zero = sb("g_zero", [P, ZR * (F + 1)])
        g_src = sb("g_src", [P, 1], I32)
        g_dst = sb("g_dst", [P, 1], I32)
        g_xs = sb("g_xs", [P, F])
        g_xd = sb("g_xd", [P, F])
        g_theta = sb("g_theta", [P, F])
        g_thetaT = sb("g_thetaT", [P, P])
        g_hidden = sb("g_hidden", [P, P])
        g_wgt = sb("g_wgt", [P, 1])
        g_dst_f = sb("g_dst_f", [P, 1])
        g_same = sb("g_same", [P, P])
        g_earlier = sb("g_earlier", [P, P])
        g_dup = sb("g_dup", [P, 1])
        g_shift = sb("g_shift", [P, 1])
        g_to_f = sb("g_to_f", [P, 1])
        g_to = sb("g_to", [P, 1], I32)
        g_terms = sb("g_terms", [P, F + 1])
        g_rows = sb("g_rows", [P, F + 1])
        g_acc = sb("g_acc", [P, F + 1])
        g_x = sb("g_x", [P, F])
        g_xT = sb("g_xT", [P, P])
        g_lin = sb("g_lin", [P, F])
        g_mix = sb("g_mix", [P, F])
        spare_row = sb("spare_row", [P, 1])
        flag_f = sb("flag_f", [P, 4])
        flag = sb("flag", [P, 1], I32)

        ps_rel = ps("ps_rel", [P, B * P])
        ps_srcT = [ps(f"ps_srcT{n}", [P, B * P]) for n in range(2)]
        ps_hid = [ps(f"ps_hid{n}", [P, B * P]) for n in range(2)]
        ps_log = ps("ps_log", [P, 512])
        ps_sum = ps("ps_sum", [P, 512])
        ps_win = ps("ps_win", [P, 512])

        const_in = sem("const_in")
        iota_done = sem("iota_done")
        const_done = sem("const_done")
        neg_ready = sem("neg_ready")
        src_in = [sem(f"src_in{n}") for n in range(2)]
        dst_in = [sem(f"dst_in{n}") for n in range(2)]
        first_in = [sem(f"first_in{n}") for n in range(2)]
        window_in = [sem(f"window_in{n}") for n in range(2)]
        gathered = [sem(f"gathered{n}") for n in range(NB)]
        base_ready = sem("base_ready")
        rel_ready = sem("rel_ready")
        parts_ready = sem("parts_ready")
        rel_spread = sem("rel_spread")
        hot_ready = sem("hot_ready")
        hid_dst = sem("hid_dst")
        srcT_ready = sem("srcT_ready")
        srcT_copied = sem("srcT_copied")
        hid_ready = sem("hid_ready")
        relu_ready = sem("relu_ready")
        logit_ready = sem("logit_ready")
        wgt_ready = sem("wgt_ready")
        hotw_ready = sem("hotw_ready")
        summed = sem("summed")
        sums_out = sem("sums_out")
        winT_ready = sem("winT_ready")
        winT_copied = sem("winT_copied")
        win_ready = sem("win_ready")
        win_read = sem("win_read")
        y_ready = sem("y_ready")
        y_out = sem("y_out")
        stored = sem("stored")
        prep_chain = sem("prep_chain")
        split_chain = sem("split_chain")
        check_chain = sem("check_chain")
        sum_chain = sem("sum_chain")
        rows_chain = sem("rows_chain")
        norm_chain = sem("norm_chain")
        carry_ready = sem("carry_ready")
        end_chain = sem("end_chain")
        total_ready = sem("total_ready")
        flag_ready = sem("flag_ready")
        g_cleared = sem("g_cleared")
        g_tile = sem("g_tile")
        g_ids_in = [sem(f"g_ids_in{n}") for n in range(GU)]
        g_x_in = [sem(f"g_x_in{n}") for n in range(GU)]
        g_added = [sem(f"g_added{n}") for n in range(GU)]
        g_node_in = [sem(f"g_node_in{n}") for n in range(GU)]
        g_node_out = [sem(f"g_node_out{n}") for n in range(GU)]
        (g_theta_ready, g_thetaT_ready, g_thetaT_copied, g_hid_ready, g_relu_ready, g_logit_ready,
         g_wgt_ready, g_terms_ready, g_dst_ready, g_spread, g_same_ready, g_to_ready, g_sum_ready,
         g_rows_ready, g_xT_ready, g_xT_copied, g_lin_ready, g_y_ready, g_chain, gn_chain) = [
            sem(name) for name in (
                "g_theta_ready", "g_thetaT_ready", "g_thetaT_copied", "g_hid_ready", "g_relu_ready",
                "g_logit_ready", "g_wgt_ready", "g_terms_ready", "g_dst_ready", "g_spread",
                "g_same_ready", "g_to_ready", "g_sum_ready", "g_rows_ready", "g_xT_ready",
                "g_xT_copied", "g_lin_ready", "g_y_ready", "g_chain", "gn_chain")]
        sp_gate = sem("sp_gate")
        pool_gate = sem("pool_gate")
        dve_gate = sem("dve_gate")

        def all_chunks(body, eng):
            body(Chunk(0, 0, 1), NB)
            with eng.Fori(0, (z.chunks - 3) // 2) as i:
                body(Chunk(i * 2 + 1, 1, i + 1), NB)
                body(Chunk(i * 2 + 2, 0, i + 2), NB)
            body(Chunk(z.chunks - 2, 1, (z.chunks - 1) // 2), NB)
            body(Chunk(z.chunks - 1, 0, (z.chunks + 1) // 2), NB)
            body(Chunk(z.chunks, 1, (z.chunks + 1) // 2), 1)

        def nxt(k):
            return Chunk(k.c + 1, 1 - k.parity, k.nth + k.parity)

        def pair(k, j):
            return (k.parity + j) % 2

        def prv(k):
            return Chunk(k.c - 1, 1 - k.parity, k.nth - 1 + k.parity)

        def is_first(k):
            return isinstance(k.c, int) and k.c == 0

        def is_last(k):
            return isinstance(k.c, int) and k.c == z.chunks

        def at(k, j, batches=NB):
            if j < 0:
                return None if is_first(k) else (prv(k), j + NB)
            if j >= batches:
                return None if is_last(k) else (nxt(k), j - batches)
            return k, j

        CARRY_STEP = 2
        PREP_STEP = 3
        NORM_STEP = 4
        WIN_STEP = 4

        def load_chunk(sp, k):
            q = k.parity
            if is_last(k):
                n, lo = z.tail_parts, z.chunks * CHUNK
                cut, kk = slice(lo, z.edges), B
                one = slice(lo, lo + 1)
            else:
                n, kk = P, K
                cut, one = bass.ds(k.c * CHUNK, CHUNK), bass.ds(k.c * CHUNK, 1)
            sp.dma_start(src_i[0:n, q, 0:kk], src[cut].rearrange("(p k) -> p k", k=kk)).then_inc(src_in[q], 16)
            sp.dma_start(dst_i[0:n, q, 0:kk], dst[cut].rearrange("(p k) -> p k", k=kk)).then_inc(dst_in[q], 16)
            sp.dma_start(first_i[:, q, :], dst[one].rearrange("(a o) -> a o", a=1).to_broadcast([P, 1]))\
                .then_inc(first_in[q], 16)

        def load_window(sp, k):
            wait(sp, base_ready, k.c + 1)
            sp.sem_inc(sp_gate, 1)
            base = sp.value_load(base_i[0:1, k.parity, :], min_val=0, max_val=z.last_base)
            sp.dma_start(window[:, k.parity, :], x[bass.ds(base, P), :]).then_inc(window_in[k.parity], 16)

        def store_result(sp, k):
            wait(sp, y_ready, k.c + 1)
            sp.sem_inc(sp_gate, 1)
            base = sp.value_load(out_base[0:1, k.parity, :], min_val=0, max_val=z.last_base)
            sp.dma_start(out[bass.ds(base, P), :], yout[:, :]).then_inc(y_out, 16)
            wait(sp, y_out, 16 * (k.c + 1))
            sp.sem_inc(stored, 1)

        def windows_sync(sp):
            first = Chunk(0, 0, 1)
            load_chunk(sp, first)
            for to, what in ((w14[:, 0:F], W1), (w14[:, F:2 * F], W4), (w2[:, :], W2),
                             (b1_col[:, :], b1.rearrange("(p a) -> p a", a=1)),
                             (b2_col[:, :], b2.rearrange("(a o) -> a o", a=1).to_broadcast([P, 1])),
                             (b4_rows[:, :], b4.rearrange("(a o) -> a o", a=1).to_broadcast([P, F]))):
                sp.dma_start(to, what).then_inc(const_in, 16)
            load_window(sp, first)

            def body(k, batches):
                if not is_last(k):
                    wait(sp, summed, k.c * NB)
                    load_chunk(sp, nxt(k))
                if not is_last(k):
                    load_window(sp, nxt(k))
                if not is_first(k):
                    store_result(sp, prv(k))

            all_chunks(body, sp)
            store_result(sp, Chunk(z.chunks, 1, (z.chunks + 1) // 2))

        def windows_gpsimd(pool):
            pool.wait_ge(const_done, 1)
            def body(k, batches):
                parts = z.tail_parts if is_last(k) else P
                pool.wait_ge(src_in[k.parity], 16 * k.nth)
                pool.sem_inc(pool_gate, 1)
                for j in range(batches):
                    if not is_first(k):
                        pool.wait_ge(summed, (k.c - 1) * NB + j + 1)
                        pool.sem_inc(pool_gate, 1)
                    for t in range(j * B, (j + 1) * B):
                        nc.gpsimd.indirect_dma_start(
                            gath[0:parts, t, 0:F], None, x,
                            bass.IndirectOffsetOnAxis(ap=src_i[0:parts, k.parity, t:t + 1], axis=0))\
                            .then_inc(gathered[j], 16)

            all_chunks(body, pool)

        def windows_tensor(pe):
            def spread(k, j):
                wait(pe, hot_ready, k.c * NB + j)
                for t in range(B):
                    e = j * B + t
                    last = nc.tensor.matmul(ps_rel[:, t * P:(t + 1) * P],
                                            rel_bf[:, k.parity, e:e + 1].to_broadcast([P, P]),
                                            ident_bf[:, :], start=True, stop=True)
                last.then_inc(rel_spread, 1)

            def hidden_dst(k, j):
                b = pair(k, j)
                wait(pe, relu_ready, k.c * NB + j - 1)
                wait(pe, hot_ready, k.c * NB + j + 1)
                for m in range(3):
                    last = nc.tensor.matmul(ps_hid[b][:, :], part[:, k.parity, m, :], hot_ne[:, b, :],
                                            start=(m == 0), stop=False)
                last.then_inc(hid_dst, 1)

            def transpose_src(k, j):
                b = pair(k, j)
                wait(pe, srcT_copied, k.c * NB + j - 1)
                wait(pe, gathered[j], 16 * B * (k.c + 1))
                for t in range(B):
                    last = nc.tensor.transpose(ps_srcT[b][:, t * P:(t + 1) * P], gath[:, j * B + t, 0:F],
                                               ident[:, :])
                last.then_inc(srcT_ready, 1)

            def hidden_src(k, j):
                b = pair(k, j)
                wait(pe, srcT_copied, k.c * NB + j + 1)
                nc.tensor.matmul(ps_hid[b][:, :], neg_w1[:, :], srcT[:, b, :], start=False, stop=True)\
                    .then_inc(hid_ready, 1)

            def logits(k, j):
                b = pair(k, j)
                wait(pe, wgt_ready, k.c * NB + j)
                wait(pe, relu_ready, k.c * NB + j + 1)
                for t in range(B):
                    last = nc.tensor.matmul(ps_log[:, t:t + 1],
                                            hidden[:, b, t * P:(t + 1) * P], w2[:, :], start=True, stop=True)
                last.then_inc(logit_ready, 1)

            def carry(k):
                wait(pe, carry_ready, k.c + 1)
                wait(pe, sums_out, k.c + 1)
                nc.tensor.matmul(ps_sum[:, 0:F + 2], carry_sel[:, k.parity, :], sums[:, :], start=True, stop=False)

            def add_up(k, j, stop):
                b = pair(k, j)
                wait(pe, hotw_ready, k.c * NB + j + 1)
                for t in range(B):
                    last = nc.tensor.matmul(ps_sum[:, 0:F + 1], hot_en[:, b, t, :],
                                            gath[:, j * B + t, 0:F + 1],
                                            start=False, stop=(stop and t == B - 1))
                last.then_inc(summed, 1)

            def transpose_window(k):
                wait(pe, win_read, k.c)
                wait(pe, window_in[k.parity], 16 * k.nth)
                nc.tensor.transpose(ps_win[:, 2 * F:2 * F + P], window[:, k.parity, :], ident[:, :])\
                    .then_inc(winT_ready, 1)

            def project_window(k):
                wait(pe, winT_copied, k.c + 1)
                nc.tensor.matmul(ps_win[:, 0:2 * F], winT[:, :], w14[:, :], start=True, stop=True)\
                    .then_inc(win_ready, 1)

            def body(k, batches):
                for s in range(batches if batches == NB else CARRY_STEP + batches):
                    ahead, now = at(k, s + 1, batches), (s < batches)
                    if now and ahead:
                        if ahead[1] == 0:
                            wait(pe, rel_ready, ahead[0].c + 1)
                        spread(*ahead)
                    if now:
                        if s == 0:
                            wait(pe, parts_ready, k.c + 1)
                        hidden_dst(k, s)
                    if now:
                        transpose_src(k, s)
                    if s - 1 < batches and at(k, s - 1):
                        logits(*at(k, s - 1))
                    if s == WIN_STEP:
                        transpose_window(nxt(k))
                    if s == CARRY_STEP:
                        carry(k)
                    if at(k, s - 2):
                        done, j = at(k, s - 2)
                        add_up(done, j, j == NB - 1 or is_last(done))
                    if now:
                        hidden_src(k, s)
                    if s == WIN_STEP:
                        project_window(nxt(k))

            transpose_window(Chunk(0, 0, 1))
            pe.wait_ge(const_in, 16 * 6)
            pe.wait_ge(neg_ready, 1)
            project_window(Chunk(0, 0, 1))
            pe.wait_ge(rel_ready, 1)
            spread(Chunk(0, 0, 1), 0)
            all_chunks(body, pe)

        def windows_scalar(act):
            def copy_src(k, j):
                b = pair(k, j)
                wait(act, hid_ready, k.c * NB + j - 1)
                wait(act, srcT_ready, k.c * NB + j + 1)
                nc.scalar.copy(srcT[:, b, :], ps_srcT[b][:, :]).then_inc(srcT_copied, 1)

            def relu(k, j):
                b = pair(k, j)
                wait(act, logit_ready, k.c * NB + j - 1)
                wait(act, hid_ready, k.c * NB + j + 1)
                nc.scalar.activation(hidden[:, b, :], ps_hid[b][:, :], ACT.Relu, bias=b1_col[:, :])\
                    .then_inc(relu_ready, 1)

            def gate(k, j):
                b = pair(k, j)
                wait(act, hotw_ready, k.c * NB + j - 1)
                wait(act, logit_ready, k.c * NB + j + 1)
                nc.scalar.activation(wgt[:, b, :], ps_log[:, 0:B], ACT.Sigmoid,
                                     bias=b2_col[:, :]).then_inc(wgt_ready, 1)

            def copy_window(k):
                wait(act, winT_ready, k.c + 1)
                nc.scalar.copy(winT[:, :], ps_win[:, 2 * F:2 * F + P]).then_inc(winT_copied, 1)

            def body(k, batches):
                for j in range(batches if batches == NB else batches + 1):
                    if j < batches:
                        copy_src(k, j)
                    if at(k, j - 1):
                        gate(*at(k, j - 1))
                    if j == WIN_STEP:
                        copy_window(nxt(k))
                    if j < batches:
                        relu(k, j)

            copy_window(Chunk(0, 0, 1))
            act.wait_ge(const_in, 16 * 6)
            all_chunks(body, act)

        def inverse_root(link):
            v = nc.vector
            link(v.tensor_scalar(var[:, :], mv[:, 1:2], EPS, None, ALU.add))
            v.tensor_scalar(neg_half[:, :], var[:, :], -0.5, None, ALU.mult)
            link(v.tensor_scalar(bits[:, :], var[:, :].bitcast(I32), 1, None, ALU.logical_shift_right))
            link(v.tensor_scalar(rstd[:, :].bitcast(I32), bits[:, :], -1.0, float(0x5F3759DF), ALU.mult, ALU.add))
            for _ in range(3):
                link(v.scalar_tensor_tensor(square[:, :], rstd[:, :], rstd[:, :], neg_half[:, :],
                                            ALU.mult, ALU.mult))
                link(v.scalar_tensor_tensor(rstd[:, :], square[:, :], 1.5, rstd[:, :], ALU.add, ALU.mult))

        PREP, CHECK, SPLIT, SUM, ROWS, NORM = 3, 5, 3, 1, 6, 9

        def windows_vector(dve):
            def prepare(k):
                q, n, kk = (k.parity, z.tail_parts, B) if is_last(k) else (k.parity, P, K)
                link = Chain(dve, prep_chain, k.c * PREP)
                wait(dve, first_in[q], 16 * k.nth)
                link(nc.vector.tensor_scalar(base_i[:, q, :], first_i[:, q, :], z.last_base, None, ALU.min))
                link(nc.vector.tensor_copy(base_f[:, q, :], base_i[:, q, :]))
                dve.sem_inc(base_ready, 1)
                wait(dve, dst_in[q], 16 * k.nth)
                if is_last(k):
                    nc.vector.memset(rel[:, q, :], -1.0).then_inc(end_chain, 1)
                    dve.wait_ge(end_chain, 1)
                link(nc.vector.tensor_scalar(rel[0:n, q, 0:kk], dst_i[0:n, q, 0:kk], base_f[0:n, q, :], None,
                                             ALU.subtract))
                nc.vector.tensor_copy(rel_bf[:, q, :], rel[:, q, :]).then_inc(rel_ready, 1)

            def compare_windows(k):
                q = k.parity
                link = Chain(dve, check_chain, k.c * CHECK)
                link(nc.vector.tensor_tensor(delta[:, :], base_f[:, 1 - q, :], base_f[:, q, :], ALU.subtract))
                nc.vector.tensor_tensor(carry_sel[:, q, :], col_minus_row[:, :],
                                        delta[:, :].to_broadcast([P, P]), ALU.is_equal).then_inc(carry_ready, 1)
                link(nc.vector.tensor_scalar(step_back[:, :], delta[:, :], 0.0, None, ALU.is_gt))
                link(nc.vector.tensor_scalar(step_far[:, :], delta[:, :], -float(P), None, ALU.is_lt))
                link(nc.vector.tensor_tensor(step_back[:, :], step_back[:, :], step_far[:, :], ALU.add))
                link(nc.vector.tensor_tensor(bad[:, :], bad[:, :], step_back[:, :], ALU.add))

            def split(k):
                q = k.parity
                link = Chain(dve, split_chain, k.c * SPLIT)
                wait(dve, win_ready, k.c + 1)
                rows = ps_win[:, 0:F]
                link(nc.vector.tensor_copy(part[:, q, 0, :], rows))
                nc.vector.tensor_tensor(rest[:, :], rows, part[:, q, 0, :], ALU.subtract)
                link(nc.vector.tensor_tensor(part[:, q, 1, :], rows, part[:, q, 0, :], ALU.subtract))
                link(nc.vector.tensor_tensor(part[:, q, 2, :], rest[:, :], part[:, q, 1, :], ALU.subtract))
                nc.vector.tensor_tensor(lin[:, q, :], ps_win[:, F:2 * F], b4_rows[:, :], ALU.add)\
                    .then_inc(win_read, 1)
                dve.sem_inc(parts_ready, 1)

            def one_hot(k, j):
                b = pair(k, j)
                wait(dve, rel_spread, k.c * NB + j + 1)
                wait(dve, hid_dst, k.c * NB + j - 1)
                nc.vector.tensor_scalar(hot_ne[:, b, :], ps_rel[:, :], row_no[:, :], None, ALU.is_equal,
                                        ALU.add, accum_out=deg[:, k.parity, j:j + 1]).then_inc(hot_ready, 1)

            def weighted(k, j):
                b = pair(k, j)
                wait(dve, wgt_ready, k.c * NB + j + 1)
                wait(dve, summed, k.c * NB + j - 1)
                for t in range(B):
                    e = j * B + t
                    last = nc.vector.scalar_tensor_tensor(hot_en[:, b, t, :], col_no[:, :],
                                                          rel[:, k.parity, e:e + 1],
                                                          wgt[:, b, t:t + 1].to_broadcast([P, P]),
                                                          ALU.is_equal, ALU.mult)
                last.then_inc(hotw_ready, 1)

            def take_sums(k, batches):
                link = Chain(dve, sum_chain, k.c * SUM)
                wait(dve, summed, k.c * NB + batches)
                link(nc.vector.tensor_reduce(deg_own[:, :], deg[:, k.parity, 0:batches], AX.X, ALU.add))
                nc.vector.tensor_tensor(placed[:, :], placed[:, :], deg_own[:, :], ALU.add)
                nc.vector.tensor_copy(sums[:, 0:F + 1], ps_sum[:, 0:F + 1])
                nc.vector.tensor_tensor(sums[:, F + 1:F + 2], ps_sum[:, F + 1:F + 2], deg_own[:, :], ALU.add)\
                    .then_inc(sums_out, 1)

            def finish_rows(k):
                link = Chain(dve, rows_chain, k.c * ROWS)
                dve.wait_ge(sums_out, k.c + 2)
                link(nc.vector.tensor_scalar(sw1[:, :], sums[:, F:F + 1], 1.0, None, ALU.add))
                link(nc.vector.scalar_tensor_tensor(mix[:, :], window[:, k.parity, :], sw1[:, :],
                                                    sums[:, 0:F], ALU.mult, ALU.subtract))
                link(nc.vector.scalar_tensor_tensor(y[:, :], lin[:, k.parity, :], sums[:, F + 1:F + 2],
                                                    mix[:, :], ALU.mult, ALU.add))
                link(nc.vector.bn_stats(stats[:, :], y[:, :]))
                dve.sem_inc(dve_gate, 1)
                link(nc.vector.bn_aggr(mv[:, :], stats[:, :]))
                link(nc.vector.tensor_copy(out_base[:, k.parity, :], base_i[:, k.parity, :]))

            def normalise(k):
                link = Chain(dve, norm_chain, k.c * NORM)
                inverse_root(link)
                dve.sem_inc(dve_gate, 1)
                dve.wait_ge(stored, k.c + 1)
                nc.vector.scalar_tensor_tensor(yout[:, :], y[:, :], mv[:, 0:1], rstd[:, :].to_broadcast([P, F]),
                                               ALU.subtract, ALU.mult).then_inc(y_ready, 1)

            def body(k, batches):
                for j in range(batches if batches == NB else CARRY_STEP + 1):
                    if j < batches and at(k, j + 1, batches):
                        one_hot(*at(k, j + 1, batches))
                    if j == CARRY_STEP and not is_first(k):
                        take_sums(prv(k), NB)
                    if j == PREP_STEP:
                        prepare(nxt(k))
                    if j - 1 < batches and at(k, j - 1):
                        weighted(*at(k, j - 1))
                    if j == CARRY_STEP and not is_first(k):
                        finish_rows(prv(k))
                        if is_last(k):
                            normalise(prv(k))
                    if j == NORM_STEP and not is_first(k):
                        normalise(prv(k))
                    if j == WIN_STEP + 1:
                        split(nxt(k))
                    if j == NB - 1:
                        compare_windows(nxt(k))

            first, last = Chunk(0, 0, 1), Chunk(z.chunks, 1, (z.chunks + 1) // 2)
            prepare(first)
            compare_windows(first)
            dve.wait_ge(const_in, 16 * 6)
            nc.vector.tensor_scalar(neg_w1[:, :], w14[:, 0:F], -1.0, None, ALU.mult).then_inc(neg_ready, 1)
            split(first)
            one_hot(first, 0)
            all_chunks(body, dve)
            take_sums(last, 1)
            finish_rows(last)
            normalise(last)

        def constants_gpsimd(pool):
            nc.gpsimd.iota(col_no[:, :], [[1, P]], base=0, channel_multiplier=0,
                           allow_small_or_imprecise_dtypes=True).then_inc(iota_done, 1)
            nc.gpsimd.iota(col_minus_row[:, :], [[1, P]], base=0, channel_multiplier=-1,
                           allow_small_or_imprecise_dtypes=True).then_inc(iota_done, 1)
            nc.gpsimd.iota(row_no[:, :], [[0, 1]], base=0, channel_multiplier=1,
                           allow_small_or_imprecise_dtypes=True).then_inc(iota_done, 1)

        def constants_vector(dve):
            dve.wait_ge(iota_done, 3)
            v = nc.vector
            v.tensor_scalar(ident[:, :], col_minus_row[:, :], 0.0, None, ALU.is_equal)
            v.tensor_scalar(ident_bf[:, :], col_minus_row[:, :], 0.0, None, ALU.is_equal)
            v.tensor_scalar(before[:, :], col_minus_row[:, :], 0.0, None, ALU.is_lt)
            v.memset(ones_col[:, :], 1.0)
            v.memset(gath[:, :, F:F + 1], 1.0)
            v.memset(sums[:, :], 0.0).then_inc(sums_out, 1)
            v.memset(placed[:, :], 0.0).then_inc(stored, 1)
            v.memset(g_zero[:, :], 0.0)
            v.memset(g_terms[:, F:F + 1], 1.0)
            v.tensor_scalar(spare_row[:, :], row_no[:, :], float(z.nodes), None, ALU.add)
            v.memset(base_f[:, 1, :], -float(P))
            v.memset(bad[:, :], 0.0).then_inc(const_done, 1)
            dve.wait_ge(const_done, 1)

        def check_tensor(pe):
            wait(pe, sums_out, z.chunks + 2)
            nc.tensor.matmul(ps_log[0:1, 0:1], placed[:, :], ones_col[:, :], start=True, stop=True)\
                .then_inc(total_ready, 1)

        def check_vector(dve):
            link = Chain(dve, end_chain, 1)
            q = z.chunks % 2
            dve.wait_ge(total_ready, 1)
            link(nc.vector.tensor_scalar(flag_f[0:1, 0:1], ps_log[0:1, 0:1], float(z.edges), None, ALU.not_equal))
            link(nc.vector.tensor_tensor(flag_f[0:1, 1:2], flag_f[0:1, 0:1], bad[0:1, :], ALU.add))
            link(nc.vector.tensor_scalar(flag_f[0:1, 2:3], base_f[0:1, q, :], float(z.last_base), None,
                                         ALU.not_equal))
            link(nc.vector.tensor_tensor(flag_f[0:1, 3:4], flag_f[0:1, 1:2], flag_f[0:1, 2:3], ALU.add))
            link(nc.vector.tensor_scalar(flag_f[0:1, 3:4], flag_f[0:1, 3:4], 1.0, None, ALU.min))
            nc.vector.tensor_copy(flag[0:1, :], flag_f[0:1, 3:4]).then_inc(flag_ready, 1)

        G, tiles = z.gp, z.edge_turns * GU

        def edge_tiles(eng, tile):
            with eng.Fori(0, z.edge_turns) as i:
                for u in range(GU):
                    tile(i * GU + u, i, u)

        def node_tiles(eng, tile):
            with eng.Fori(0, z.node_tiles // GU) as i:
                for u in range(GU):
                    tile(i * GU + u, i, u)

        def general_sync(sp):
            sp.wait_ge(const_done, 1)
            per = z.nodes // G
            assert per % ZR == 0
            flat = acc[0:z.nodes, :].rearrange("(p j) f -> p (j f)", p=G)
            for n in range(per // ZR):
                w = ZR * (F + 1)
                sp.dma_start(flat[:, n * w:(n + 1) * w], g_zero[0:G, :]).then_inc(g_cleared, 16)
            sp.dma_start(acc[z.nodes:z.nodes + P, :], g_zero[:, 0:F + 1]).then_inc(g_cleared, 16)
            sp.wait_ge(g_cleared, 16 * (per // ZR + 1))
            sp.sem_inc(g_tile, 1)

            def edge(t, i, u):
                sp.wait_ge(g_tile, t + 1)
                sp.dma_start(g_src[0:G, :], src[bass.ds(t * G, G)].rearrange("(p a) -> p a", a=1))\
                    .then_inc(g_ids_in[u], 16)
                sp.dma_start(g_dst[0:G, :], dst[bass.ds(t * G, G)].rearrange("(p a) -> p a", a=1))\
                    .then_inc(g_ids_in[u], 16)

            def node(n, i, u):
                sp.dma_start(g_acc[0:G, :], acc[bass.ds(n * G, G), :]).then_inc(g_node_in[u], 16)
                sp.dma_start(g_x[0:G, :], x[bass.ds(n * G, G), :]).then_inc(g_node_in[u], 16)
                sp.wait_ge(g_y_ready, n + 1)
                sp.dma_start(out[bass.ds(n * G, G), :], yout[0:G, :]).then_inc(g_node_out[u], 16)
                sp.wait_ge(g_node_out[u], 16 * (i + 1))
                sp.sem_inc(sp_gate, 1)

            edge_tiles(sp, edge)
            sp.wait_ge(g_tile, tiles + 1)
            node_tiles(sp, node)

        def general_gpsimd(pool):
            def edge(t, i, u):
                pool.wait_ge(g_ids_in[u], 32 * (i + 1))
                pool.sem_inc(pool_gate, 1)
                for to, ids in ((g_xs, g_src), (g_xd, g_dst)):
                    nc.gpsimd.indirect_dma_start(to[0:G, :], None, x,
                                                 bass.IndirectOffsetOnAxis(ap=ids[0:G, :], axis=0))\
                        .then_inc(g_x_in[u], 16)
                pool.wait_ge(g_rows_ready, t + 1)
                pool.sem_inc(pool_gate, 1)
                nc.gpsimd.indirect_dma_start(acc, bass.IndirectOffsetOnAxis(ap=g_to[0:G, :], axis=0),
                                             g_rows[0:G, :], None, compute_op=ALU.add)\
                    .then_inc(g_added[u], 16)
                pool.wait_ge(g_added[u], 16 * (i + 1))
                pool.sem_inc(g_tile, 1)

            edge_tiles(pool, edge)

        def general_tensor(pe):
            def edge(t, i, u):
                pe.wait_ge(g_theta_ready, t + 1)
                nc.tensor.transpose(ps_srcT[0][:, 0:G], g_theta[0:G, :], ident[0:G, 0:G])\
                    .then_inc(g_thetaT_ready, 1)
                pe.wait_ge(g_dst_ready, t + 1)
                nc.tensor.matmul(ps_rel[0:G, 0:G], g_dst_f[0:G, :].to_broadcast([G, G]), ident[0:G, 0:G],
                                 start=True, stop=True).then_inc(g_spread, 1)
                pe.wait_ge(g_thetaT_copied, t + 1)
                nc.tensor.matmul(ps_hid[0][:, 0:G], w14[:, 0:F], g_thetaT[:, 0:G], start=True, stop=True)\
                    .then_inc(g_hid_ready, 1)
                pe.wait_ge(g_relu_ready, t + 1)
                nc.tensor.matmul(ps_log[0:G, 0:1], g_hidden[:, 0:G], w2[:, :], start=True, stop=True)\
                    .then_inc(g_logit_ready, 1)
                pe.wait_ge(g_same_ready, t + 1)
                pe.wait_ge(g_terms_ready, t + 1)
                nc.tensor.matmul(ps_sum[0:G, 0:F + 1], g_same[0:G, 0:G], g_terms[0:G, :],
                                 start=True, stop=True).then_inc(g_sum_ready, 1)

            def node(n, i, u):
                pe.wait_ge(g_node_in[u], 32 * (i + 1))
                nc.tensor.transpose(ps_srcT[0][:, 0:G], g_x[0:G, :], ident[0:G, 0:G]).then_inc(g_xT_ready, 1)
                pe.wait_ge(g_xT_copied, n + 1)
                nc.tensor.matmul(ps_win[0:G, 0:F], g_xT[:, 0:G], w14[:, F:2 * F], start=True, stop=True)\
                    .then_inc(g_lin_ready, 1)

            edge_tiles(pe, edge)
            node_tiles(pe, node)

        def general_scalar(act):
            def edge(t, i, u):
                act.wait_ge(g_thetaT_ready, t + 1)
                nc.scalar.copy(g_thetaT[:, 0:G], ps_srcT[0][:, 0:G]).then_inc(g_thetaT_copied, 1)
                act.wait_ge(g_hid_ready, t + 1)
                nc.scalar.activation(g_hidden[:, 0:G], ps_hid[0][:, 0:G], ACT.Relu, bias=b1_col[:, :])\
                    .then_inc(g_relu_ready, 1)
                act.wait_ge(g_logit_ready, t + 1)
                nc.scalar.activation(g_wgt[0:G, :], ps_log[0:G, 0:1], ACT.Sigmoid, bias=b2_col[0:G, :])\
                    .then_inc(g_wgt_ready, 1)

            def node(n, i, u):
                act.wait_ge(g_xT_ready, n + 1)
                nc.scalar.copy(g_xT[:, 0:G], ps_srcT[0][:, 0:G]).then_inc(g_xT_copied, 1)

            edge_tiles(act, edge)
            node_tiles(act, node)

        def general_vector(dve):
            EDGE, NODE = 4, 14
            v = nc.vector

            def edge(t, i, u):
                link = Chain(dve, g_chain, t * EDGE)
                dve.wait_ge(g_x_in[u], 32 * (i + 1))
                v.tensor_tensor(g_theta[0:G, :], g_xd[0:G, :], g_xs[0:G, :], ALU.subtract)\
                    .then_inc(g_theta_ready, 1)
                v.tensor_copy(g_dst_f[0:G, :], g_dst[0:G, :]).then_inc(g_dst_ready, 1)
                dve.wait_ge(g_dst_ready, t + 1)
                dve.wait_ge(g_spread, t + 1)
                v.tensor_scalar(g_same[0:G, 0:G], ps_rel[0:G, 0:G], g_dst_f[0:G, :], None, ALU.is_equal)\
                    .then_inc(g_same_ready, 1)
                dve.wait_ge(g_same_ready, t + 1)
                link(v.tensor_tensor(g_earlier[0:G, 0:G], g_same[0:G, 0:G], before[0:G, 0:G], ALU.mult))
                link(v.tensor_reduce(g_dup[0:G, :], g_earlier[0:G, 0:G], AX.X, ALU.max))
                link(v.tensor_tensor(g_shift[0:G, :], spare_row[0:G, :], g_dst_f[0:G, :], ALU.subtract))
                link(v.scalar_tensor_tensor(g_to_f[0:G, :], g_shift[0:G, :], g_dup[0:G, :], g_dst_f[0:G, :],
                                            ALU.mult, ALU.add))
                v.tensor_copy(g_to[0:G, :], g_to_f[0:G, :]).then_inc(g_to_ready, 1)
                dve.wait_ge(g_theta_ready, t + 1)
                dve.wait_ge(g_wgt_ready, t + 1)
                v.tensor_scalar(g_terms[0:G, 0:F], g_theta[0:G, :], g_wgt[0:G, :], None, ALU.mult)\
                    .then_inc(g_terms_ready, 1)
                dve.wait_ge(g_to_ready, t + 1)
                dve.wait_ge(g_sum_ready, t + 1)
                v.tensor_copy(g_rows[0:G, :], ps_sum[0:G, 0:F + 1]).then_inc(g_rows_ready, 1)

            def node(n, i, u):
                link = Chain(dve, gn_chain, n * NODE)
                dve.wait_ge(g_node_in[u], 32 * (i + 1))
                link(v.tensor_tensor(g_mix[0:G, :], g_x[0:G, :], g_acc[0:G, 0:F], ALU.add))
                dve.wait_ge(g_lin_ready, n + 1)
                link(v.tensor_tensor(g_lin[0:G, :], ps_win[0:G, 0:F], b4_rows[0:G, :], ALU.add))
                link(v.scalar_tensor_tensor(y[0:G, :], g_lin[0:G, :], g_acc[0:G, F:F + 1], g_mix[0:G, :],
                                            ALU.mult, ALU.add))
                link(v.bn_stats(stats[0:G, :], y[0:G, :]))
                dve.sem_inc(dve_gate, 1)
                link(v.bn_aggr(mv[0:G, :], stats[0:G, :]))
                inverse_root(link)
                v.tensor_scalar(yout[0:G, :], y[0:G, :], mv[0:G, 0:1], rstd[0:G, :],
                                ALU.subtract, ALU.mult).then_inc(g_y_ready, 1)

            edge_tiles(dve, edge)
            node_tiles(dve, node)

        def unless_placed(eng, general):
            eng.wait_ge(flag_ready, 1)
            asked = eng.value_load(flag[0:1, :], min_val=0, max_val=1)
            with eng.If(asked > 0):
                general(eng)

        block = ctx.enter_context(nc.Block())

        @block.sync
        def _(sp):
            windows_sync(sp)
            unless_placed(sp, general_sync)

        @block.gpsimd
        def _(pool):
            constants_gpsimd(pool)
            windows_gpsimd(pool)
            unless_placed(pool, general_gpsimd)

        @block.tensor
        def _(pe):
            pe.wait_ge(const_done, 1)
            windows_tensor(pe)
            check_tensor(pe)
            unless_placed(pe, general_tensor)

        @block.scalar
        def _(act):
            act.wait_ge(const_done, 1)
            windows_scalar(act)
            unless_placed(act, general_scalar)

        @block.vector
        def _(dve):
            constants_vector(dve)
            windows_vector(dve)
            check_vector(dve)
            unless_placed(dve, general_vector)


_INS = ["x", "src", "dst", "L0_gnn_W1", "L0_gnn_b1", "L0_gnn_W2", "L0_gnn_b2", "L0_gnn_W4", "L0_gnn_b4"]


def kernel(**inputs):
    import numpy as _np
    import concourse.bacc as _bacc
    from concourse import mybir as _mybir
    from concourse.bass_utils import run_bass_kernel_spmd as _run

    nc = _bacc.Bacc("TRN2", target_bir_lowering=False, num_devices=1)
    arrays, args = {}, []
    for name in _INS:
        a = _np.ascontiguousarray(inputs[name])
        arrays[f"in_{name}"] = a
        args.append(nc.dram_tensor(f"in_{name}", a.shape, _mybir.dt.from_np(a.dtype), kind="ExternalInput").ap())
    out = nc.dram_tensor("out", arrays["in_x"].shape, _mybir.dt.float32, kind="ExternalOutput").ap()
    build(nc, *args, out)
    r = _run(nc, [arrays], core_ids=[0])
    return r.results[0]["out"]
```
